# Optimizing a Trainium2 kernel written in Bass

```python
import numpy as np
import jax
import jax.numpy as jnp

def _softmax(x, axis=-1):
    return jax.nn.softmax(x, axis=axis)

def _gelu(x):
    return jax.nn.gelu(x, approximate=True)

def _silu(x):
    return jax.nn.silu(x)

def _sigmoid(x):
    return jax.nn.sigmoid(x)

def _layernorm(x, axis=-1, eps=1e-05):
    m = jnp.mean(x, axis=axis, keepdims=True)
    v = jnp.var(x, axis=axis, keepdims=True)
    return (x - m) / jnp.sqrt(v + eps)

def _scatter_add(tgt, idx, src, axis=0):
    return tgt.at[idx].add(src)

def _segment_sum(src, seg, n):
    return jax.ops.segment_sum(src, seg, n)
kernel_name = 'mk_sandwich_d2_jaxref_r8_29ce76'

def setup_inputs(seed: int=0):
    np.random.seed(seed)
    _w = jnp.asarray

    def _L0_attn_setup():
        import jax, jax.numpy as jnp
        import numpy as np
        D_MODEL, D_STATE, DT_RANK = (128, 16, 64)
        B, L = (4, 1024)
        key = jax.random.key(seed)
        ks = jax.random.split(key, 8)
        s = 0.02
        return {'x': jax.random.normal(ks[0], (B, L, D_MODEL), dtype=jnp.float32), 'Wxproj': jax.random.normal(ks[1], (DT_RANK + 2 * D_STATE, D_MODEL), dtype=jnp.float32) * s, 'Wdt': jax.random.normal(ks[2], (1, DT_RANK), dtype=jnp.float32) * s, 'bdt': jax.random.normal(ks[3], (1,), dtype=jnp.float32) * s, 'Wxs': jax.random.normal(ks[4], (D_STATE, D_MODEL), dtype=jnp.float32) * s, 'A_log': jnp.arange(1, D_STATE + 1, dtype=jnp.float32)[None, :], 'Wout': jax.random.normal(ks[5], (D_MODEL, D_STATE), dtype=jnp.float32) * s, 'Dp': jnp.ones((D_MODEL,), dtype=jnp.float32)}
    _L0_attn_in = _L0_attn_setup()

    def _L0_ffn_setup():
        import jax, jax.numpy as jnp
        import numpy as np
        B, T, C, H, E = (4, 256, 128, 256, 8)
        CAPACITY_FACTOR = 1.0
        key = jax.random.key(seed)
        ks = jax.random.split(key, 5)
        scale = 0.02
        return {'x': jax.random.normal(ks[0], (B, T, C), dtype=jnp.float32), 'Wg': jax.random.normal(ks[1], (E, C), dtype=jnp.float32) * scale, 'W1': jax.random.normal(ks[2], (E, H, C), dtype=jnp.float32) * scale, 'W2': jax.random.normal(ks[3], (E, C, H), dtype=jnp.float32) * scale, 'W3': jax.random.normal(ks[4], (E, H, C), dtype=jnp.float32) * scale}
    _L0_ffn_in = _L0_ffn_setup()

    def _L1_attn_setup():
        import jax, jax.numpy as jnp
        import numpy as np
        DIM = 128
        DIM_HEAD = 16
        HEADS = 8
        EPS = 1e-05

        def rms_norm(x, gamma):
            n = jnp.sqrt(jnp.sum(x * x, axis=-1, keepdims=True))
            return gamma * (x / jnp.maximum(n, 1e-12)) * x.shape[-1] ** 0.5

        def second_taylor_expansion(x):
            d = x.shape[-1]
            x0 = jnp.ones(x.shape[:-1] + (1,), dtype=x.dtype)
            x2 = jnp.einsum('...i,...j->...ij', x, x) * 0.5 ** 0.5
            x2 = x2.reshape(x.shape[:-1] + (d * d,))
            return jnp.concatenate([x0, x, x2], axis=-1)
        key = jax.random.key(seed)
        ks = jax.random.split(key, 4)
        b, n = (4, 1024)
        dim_inner = DIM_HEAD * HEADS
        x = jax.random.normal(ks[0], (b, n, DIM), dtype=jnp.float32)
        gamma = jnp.ones((DIM,), dtype=jnp.float32)
        w_q = jax.random.normal(ks[1], (DIM, dim_inner), dtype=jnp.float32) * DIM ** (-0.5)
        w_kv = jax.random.normal(ks[2], (DIM, dim_inner * 2), dtype=jnp.float32) * DIM ** (-0.5)
        w_out = jax.random.normal(ks[3], (dim_inner, DIM), dtype=jnp.float32) * dim_inner ** (-0.5)
        return {'x': x, 'gamma': gamma, 'w_q': w_q, 'w_kv': w_kv, 'w_out': w_out}
    _L1_attn_in = _L1_attn_setup()

    def _L1_ffn_setup():
        import jax, jax.numpy as jnp
        import numpy as np
        D_MODEL = 128
        HIDDEN = 512
        N_EXPERTS = 8
        TOP_K = 2
        key = jax.random.key(seed)
        k_x, k_g, k_u, k_d, k_r = jax.random.split(key, 5)
        std = 0.02
        return {'x': jax.random.normal(k_x, (2, 256, D_MODEL), dtype=jnp.float32), 'Wg': jax.random.normal(k_g, (N_EXPERTS, D_MODEL, HIDDEN), dtype=jnp.float32) * std, 'Wu': jax.random.normal(k_u, (N_EXPERTS, D_MODEL, HIDDEN), dtype=jnp.float32) * std, 'Wd': jax.random.normal(k_d, (N_EXPERTS, HIDDEN, D_MODEL), dtype=jnp.float32) * std, 'Wr': jax.random.normal(k_r, (D_MODEL, N_EXPERTS), dtype=jnp.float32) * std}
    _L1_ffn_in = _L1_ffn_setup()
    _d = {'L0_attn_x': _L0_attn_in['x'], 'L0_attn_Wxproj': _L0_attn_in['Wxproj'], 'L0_attn_Wdt': _L0_attn_in['Wdt'], 'L0_attn_bdt': _L0_attn_in['bdt'], 'L0_attn_Wxs': _L0_attn_in['Wxs'], 'L0_attn_A_log': _L0_attn_in['A_log'], 'L0_attn_Wout': _L0_attn_in['Wout'], 'L0_attn_Dp': _L0_attn_in['Dp'], 'L0_ffn_Wg': _L0_ffn_in['Wg'], 'L0_ffn_W1': _L0_ffn_in['W1'], 'L0_ffn_W2': _L0_ffn_in['W2'], 'L0_ffn_W3': _L0_ffn_in['W3'], 'L1_attn_gamma': _L1_attn_in['gamma'], 'L1_attn_w_q': _L1_attn_in['w_q'], 'L1_attn_w_kv': _L1_attn_in['w_kv'], 'L1_attn_w_out': _L1_attn_in['w_out'], 'L1_ffn_Wg': _L1_ffn_in['Wg'], 'L1_ffn_Wu': _L1_ffn_in['Wu'], 'L1_ffn_Wd': _L1_ffn_in['Wd'], 'L1_ffn_Wr': _L1_ffn_in['Wr']}
    _x0 = _d['L0_attn_x']
    _d['L0_attn_x'] = jax.random.normal(jax.random.fold_in(jax.random.key(seed), 1), (2, 2048, 128), dtype=_x0.dtype)
    del _x0
    return _d

def reference(L0_attn_x, L0_attn_Wxproj, L0_attn_Wdt, L0_attn_bdt, L0_attn_Wxs, L0_attn_A_log, L0_attn_Wout, L0_attn_Dp, L0_ffn_Wg, L0_ffn_W1, L0_ffn_W2, L0_ffn_W3, L1_attn_gamma, L1_attn_w_q, L1_attn_w_kv, L1_attn_w_out, L1_ffn_Wg, L1_ffn_Wu, L1_ffn_Wd, L1_ffn_Wr):

    def _L0_attn_ref(x, Wxproj, Wdt, bdt, Wxs, A_log, Wout, Dp):
        import jax, jax.numpy as jnp
        import numpy as np
        D_MODEL, D_STATE, DT_RANK = (128, 16, 64)
        B, L = (4, 1024)
        dt_rank = Wdt.shape[1]
        N = A_log.shape[1]
        Bsz = x.shape[0]
        proj = jnp.einsum('bld,pd->blp', x, Wxproj)
        dt_part = proj[..., :dt_rank]
        B_part = proj[..., dt_rank:dt_rank + N]
        C_part = proj[..., dt_rank + N:]
        dt = jax.nn.softplus(jnp.einsum('blr,or->blo', dt_part, Wdt) + bdt)
        A = -jnp.exp(A_log)
        A_bar = jnp.exp(dt * A)
        Bx = dt * B_part * jnp.einsum('bld,nd->bln', x, Wxs)

        def step(h, inp):
            a_t, bx_t = inp
            h = a_t * h + bx_t
            return (h, h)
        h0 = jnp.zeros((Bsz, N), dtype=x.dtype)
        _, hs = jax.lax.scan(step, h0, (jnp.swapaxes(A_bar, 0, 1), jnp.swapaxes(Bx, 0, 1)))
        hc = hs * jnp.swapaxes(C_part, 0, 1)
        y = jnp.einsum('lbn,dn->bld', hc, Wout)
        return y + Dp * x

    def _L0_ffn_ref(x, Wg, W1, W2, W3):
        import jax, jax.numpy as jnp
        import numpy as np
        B, T, C, H, E = (4, 256, 128, 256, 8)
        CAPACITY_FACTOR = 1.0
        b, t, c = x.shape
        e = Wg.shape[0]
        n = b * t
        capacity = max(1, int(CAPACITY_FACTOR * n / e))
        x_flat = x.reshape(n, c)
        scores = (x_flat @ Wg.T).T
        top_vals, token_idx = jax.lax.top_k(scores, capacity)
        token_w = jax.nn.softmax(top_vals, axis=-1)
        xg = x_flat[token_idx]
        h = jax.nn.silu(jnp.einsum('eic,ehc->eih', xg, W1)) * jnp.einsum('eic,ehc->eih', xg, W3)
        y = jnp.einsum('eih,ech->eic', h, W2) * token_w[..., None]
        out = jnp.zeros_like(x_flat).at[token_idx.reshape(-1)].add(y.reshape(-1, c))
        return out.reshape(b, t, c)

    def _L1_attn_ref(x, gamma, w_q, w_kv, w_out):
        import jax, jax.numpy as jnp
        import numpy as np
        DIM = 128
        DIM_HEAD = 16
        HEADS = 8
        EPS = 1e-05

        def rms_norm(x, gamma):
            n = jnp.sqrt(jnp.sum(x * x, axis=-1, keepdims=True))
            return gamma * (x / jnp.maximum(n, 1e-12)) * x.shape[-1] ** 0.5

        def second_taylor_expansion(x):
            d = x.shape[-1]
            x0 = jnp.ones(x.shape[:-1] + (1,), dtype=x.dtype)
            x2 = jnp.einsum('...i,...j->...ij', x, x) * 0.5 ** 0.5
            x2 = x2.reshape(x.shape[:-1] + (d * d,))
            return jnp.concatenate([x0, x, x2], axis=-1)
        b, n, _ = x.shape
        h, dh = (HEADS, DIM_HEAD)
        normed = rms_norm(x, gamma)
        q = (normed @ w_q).reshape(b, n, h, dh).transpose(0, 2, 1, 3)
        kv = (normed @ w_kv).reshape(b, n, 2, h, dh).transpose(2, 0, 3, 1, 4)
        k, v = (kv[0], kv[1])
        q = q * dh ** (-0.5)
        q = second_taylor_expansion(q)
        k = second_taylor_expansion(k)
        kv_state = jnp.einsum('bhnd,bhne->bhde', k, v)
        k_sum = jnp.sum(k, axis=2)
        den = jnp.einsum('bhnd,bhd->bhn', q, k_sum)
        qk_inv = 1.0 / jnp.maximum(den, EPS)
        out = jnp.einsum('bhnd,bhde->bhne', q, kv_state) * qk_inv[..., None]
        out = out.transpose(0, 2, 1, 3).reshape(b, n, h * dh)
        return out @ w_out

    def _L1_ffn_ref(x, Wg, Wu, Wd, Wr):
        import jax, jax.numpy as jnp
        import numpy as np
        D_MODEL = 128
        HIDDEN = 512
        N_EXPERTS = 8
        TOP_K = 2
        bsz, seq_len, dim = x.shape
        flat = x.reshape(bsz * seq_len, dim)
        router_probs = jax.nn.softmax(flat @ Wr, axis=-1)
        topk_vals, topk_idx = jax.lax.top_k(router_probs, TOP_K)
        topk_vals = topk_vals / jnp.sum(topk_vals, axis=-1, keepdims=True)
        combine = jnp.sum(jax.nn.one_hot(topk_idx, N_EXPERTS, dtype=flat.dtype) * topk_vals[..., None], axis=1)
        output = jnp.zeros_like(flat)
        for e in range(N_EXPERTS):
            gated = jax.nn.silu(flat @ Wg[e]) * (flat @ Wu[e])
            output = output + combine[:, e:e + 1] * (gated @ Wd[e])
        return output.reshape(bsz, seq_len, dim)
    x = L0_attn_x
    x = x + _layernorm(_L0_attn_ref(_layernorm(x, axis=-1), L0_attn_Wxproj, L0_attn_Wdt, L0_attn_bdt, L0_attn_Wxs, L0_attn_A_log, L0_attn_Wout, L0_attn_Dp), axis=-1)
    x = x + _layernorm(_L0_ffn_ref(_layernorm(x, axis=-1), L0_ffn_Wg, L0_ffn_W1, L0_ffn_W2, L0_ffn_W3), axis=-1)
    x = x + _layernorm(_L1_attn_ref(_layernorm(x, axis=-1), L1_attn_gamma, L1_attn_w_q, L1_attn_w_kv, L1_attn_w_out), axis=-1)
    x = x + _layernorm(_L1_ffn_ref(_layernorm(x, axis=-1), L1_ffn_Wg, L1_ffn_Wu, L1_ffn_Wd, L1_ffn_Wr), axis=-1)
    return x

_drawn_inputs = setup_inputs


def setup_inputs(seed=0):
    import zlib

    import numpy as np

    out = dict(_drawn_inputs(seed))
    spreads = {'L0_attn_Dp': (1.0, 0.2), 'L1_attn_gamma': (1.0, 0.2)}
    factors = {'L0_attn_Wxproj': 8.0,
     'L0_attn_Wdt': 8.0,
     'L0_attn_Wxs': 8.0,
     'L0_attn_A_log': 61.485,
     'L0_attn_Wout': 8.0,
     'L0_ffn_Wg': 3.591,
     'L0_ffn_W1': 3.241,
     'L0_ffn_W2': 3.205,
     'L0_ffn_W3': 3.638}
    for name, (base, spread) in spreads.items():
        noise = np.random.default_rng([zlib.crc32(name.encode()), seed]).standard_normal(out[name].shape)
        drawn = base * np.exp(spread * noise) if base else spread * noise
        out[name] = jnp.asarray(drawn.astype(out[name].dtype))
    for name, factor in factors.items():
        out[name] = (out[name] * factor).astype(out[name].dtype)
    return out
```

```python
from contextlib import ExitStack

import numpy as np
import concourse.bass as bass
from concourse import mybir
from concourse.bass import ds

F32 = mybir.dt.float32
U32 = mybir.dt.uint32
I32 = mybir.dt.int32
BF16 = mybir.dt.bfloat16
ALU = mybir.AluOpType
ACT = mybir.ActivationFunctionType
AX = mybir.AxisListType

P = 128
NB, L, D = 2, 2048, 128
T = NB * L // P
TB = T // NB
CH = 4
J = TB // CH
W = J * P
NS = 16
E0, CAP, H0 = 8, NB * L // 8, 256
EPS = 1e-5
SEG = NB * L // 16
HD, DH = 8, 16
KW = 24
ND = DH // 2 + 1
E1, H1 = 8, 512
NT = 2 * NB * L // P + E1
LEAD = 1
ROWS = D + E0


class Tally:

    def __init__(self, eng, sem):
        self.eng, self.sem, self.base, self.i, self.per, self.k = eng, sem, 0, 0, 0, 0

    def begin(self, i, per):
        self.i, self.per, self.k = i, per, 0

    def end(self, trips):
        assert self.k == self.per or trips == 1, (self.k, self.per)
        self.base += trips * self.k
        self.i, self.per, self.k = 0, 0, 0

    def mark(self, ins):
        ins.then_inc(self.sem, 1)
        self.k += 1
        return self.k

    def wait(self, k=None):
        self.eng.wait_ge(self.sem, LEAD + self.i * self.per + (self.base + (self.k if k is None else k)))


def program(nc, inp, outs):
    with ExitStack() as ctx:
        def sb(name, shape, dt=F32):
            return ctx.enter_context(nc.sbuf_tensor(name, shape, dt))

        leading = []

        def sem(name):
            leading.append(ctx.enter_context(nc.semaphore(name)))
            return leading[-1]

        def sw_sem(name):
            return ctx.enter_context(nc.semaphore(name))

        bank = [ctx.enter_context(nc.psum_tensor(f"bank{i}", [P, 512], F32)) for i in range(8)]

        x1row_dram = nc.dram_tensor("x1row_dram", [T * P, ROWS], F32, kind="Internal").ap()
        score_dram = nc.dram_tensor("score_dram", [E0, T * P], F32, kind="Internal").ap()

        list_dram = nc.dram_tensor("list_dram", [E0 * CAP], I32, kind="Internal").ap()
        sum_dram = nc.dram_tensor("sum_dram", [T * P, D], F32, kind="Internal").ap()
        x3row_dram = nc.dram_tensor("x3row_dram", [T * P, D], F32, kind="Internal").ap()
        y_dram = nc.dram_tensor("y_dram", [2 * T * P + NT * P, D], F32, kind="Internal").ap()
        CON = [("wqkv", "wqkv"), ("gamma", "gamma"), ("wo", "wo"), ("wr", "wr"),
               ("tri128", "tri128"), ("iota_t", "iota_t"), ("slot_pad", "slot_pad"), ("choice128", "choice128"), ("rev8", "rev8"),
               ("wa", "wa"), ("wxp", "wxp"), ("wdt", "wdt"), ("bdt", "bdt"), ("negA", "alog"), ("wout", "wout"),
               ("dp", "dp"), ("ident", "ident"), ("wg0", "wg0"), ("blk", "blk"), ("tri", "tri"), ("bits", "bits"),
               ("iota", "iota"), ("pcol", "pcol"), ("tile128", "tile128"), ("emask", "emask")]
        NC = 16 * len(CON)

        X = sb("X", [P, NB, CH, W])
        ident = sb("ident", [P, P])
        mhalf = sb("mhalf", [P, 16])
        ones = sb("ones", [P, P])

        arena = sb("arena", [P, 14336])

        def part(at, n, dt=F32):
            v = arena[:, at:at + n]
            return v if dt == F32 else v.bitcast(dt)
        arena2 = sb("arena2", [P, 2848])

        def small(at, n):
            return arena2[:, at:at + n]
        az, ez, lz, rz, dz, dtt, abar, bx, hh, hc = (arena[0:32, k * W:(k + 1) * W] for k in range(10))

        wa = sb("wa", [P, NB, P])
        wxp = sb("wxp", [64, P])
        wdt = sb("wdt", [64, NS])
        bdt = sb("bdt", [32, 1])
        negA = sb("negA", [32, 1])
        wout = sb("wout", [32, NB, P])
        dp = sb("dp", [P, 1])
        diagD = sb("diagD", [P, P])
        st = sb("st", [P, NB, J, 6])
        mv = sb("mv", [P, NB, J, 2])
        ve = sb("ve", [P, NB, J])
        rstd = sb("rstd", [P, NB, J])
        nmr = sb("nmr", [P, NB, J])
        xnf = sb("xnf", [P, 2, 2 * W])
        xn = xnf[:, 0].rearrange("p (b j d) -> p b j d", b=NB, j=J)
        xnT = xnf[:, 1].rearrange("p (b w) -> p b w", b=NB)
        carry = sb("carry", [32, 1])
        gate = sb("gate", [P, 1])
        yn = sb("yn", [P, NB, J, P])
        fin = xnf[:].rearrange("p u (c j d) -> p u c j d", c=2, j=J)
        row = sb("row", [P, NB, J, ROWS])
        x1T = sb("x1T", [P, NB, W])
        sT = sb("sT", [E0, NB, W])
        wg0 = sb("wg0", [P, E0])

        zero = sb("zero", [P, 4, D])
        blk = sb("blk", [P, P])
        tri = sb("tri", [P, P])
        bits = sb("bits", [P, 32], U32)
        bitsf = sb("bitsf", [P, 32])
        srch = sb("srch", [P, SEG])
        hit = sb("hit", [P, SEG])
        eq = sb("eq", [P, SEG])
        rank = sb("rank", [P, SEG])
        sel = sb("sel", [P, SEG])
        onesW = sb("onesW", [P, SEG])
        iota_b = sb("iota_b", [P, P], BF16)
        qi = sb("qi", [P, 2, SEG], I32)
        qf = sb("qf", [P, 2, SEG])
        cand = sb("cand", [P, 1], U32)
        step = sb("step", [P, 1], U32)
        cntb = sb("cntb", [P, 1])
        cg = sb("cg", [P, 4])
        base = sb("base", [P, 4])
        iota = sb("iota", [P, 32])
        pcol = sb("pcol", [P, 1])
        tile128 = sb("tile128", [P, T])
        emask = sb("emask", [P, E0])
        ab = sb("ab", [P, 2, 2, P])
        oneA = part(0, 2048, BF16).rearrange("p (t e n) -> p t e n", t=T, e=E0)
        oneB = part(2048, 4096, BF16).rearrange("p (t e n) -> p t e n", t=T, e=E0)
        valP = part(6144, 4096, BF16).rearrange("p (t e n) -> p t e n", t=T, e=E0)
        valT = part(10240, 4096, BF16).rearrange("p (t e n) -> p t e n", t=T, e=E0)
        q_all = part(0, T * 192).rearrange("p (t n) -> p t n", t=T)
        prod = part(6144, 2 * ND * P).rearrange("p (u n) -> p u n", u=2)
        prodT = part(8448, 2 * 10 * P).rearrange("p (u n) -> p u n", u=2)
        sgl = part(0, 2 * H1).rearrange("p (u n) -> p u n", u=2)
        gl = part(1024, 2 * H1).rearrange("p (u n) -> p u n", u=2)
        glT = part(2048, 2 * H1).rearrange("p (u n) -> p u n", u=2)
        xr = part(3072, 4 * D).rearrange("p (u n) -> p u n", u=4)
        xrT = part(3584, 2 * D).rearrange("p (u n) -> p u n", u=2)
        yr = part(3840, 4 * D).rearrange("p (u n) -> p u n", u=4)
        oneLo2 = part(4352, P, BF16).rearrange("p (c n) -> p c n", c=2)
        oneV = part(4352 + P, 2 * NT, BF16)

        wqkv = sb("wqkv", [P, 4 * P])
        gamma = sb("gamma", [P, 1])
        wo = sb("wo", [P, P])
        wr = sb("wr", [P, E1])
        wgu = sb("wgu", [P, E1, 2 * H1])
        kvb = small(0, 642).rearrange("p (k n) -> p k n", k=2)
        zerob = sb("zerob", [P, 512], BF16)
        smat = small(642, 1280).rearrange("p (k n) -> p k n", k=ND + 1)
        kc = small(2562, 256).rearrange("p (k n) -> p k n", k=2)
        kk = small(1922, 128)
        halfblk = sb("halfblk", [P, P])
        sums = sb("sums", [P, 2])
        dt_ = part(12544, 512)
        rden = small(2050, 512)
        qst = sb("qst", [P, 2, P])
        oT = sb("oT", [P, W])
        qTg = part(13056, 512)

        tri128 = sb("tri128", [P, P])
        iota_t = sb("iota_t", [P, P])
        slot_pad = sb("slot_pad", [P, NT])
        choice128 = sb("choice128", [P, 2, T])
        rev8 = sb("rev8", [P, E1])
        lg = part(11008, 256).rearrange("p (t e) -> p t e", t=T)
        oh = part(11264, 512).rearrange("p (c t e) -> p c t e", c=2, t=T)
        tmp = part(11776, 256).rearrange("p (t e) -> p t e", t=T)
        both = part(12032, 256).rearrange("p (e t) -> p e t", e=E1)
        scan = part(12288, 256).rearrange("p (e t) -> p e t", e=E1)
        off = sb("off", [P, 4, E1])
        offi = sb("offi", [P, E1], I32)
        top = sb("top", [P, 2, T])
        wts = sb("wts", [P, 2, T])
        slot = sb("slot", [P, 2, T])
        sloti = sb("sloti", [P, 2, 2, T], I32)
        slotf = sb("slotf", [P, 2, 2, T])
        val = sb("val", [P, 2, 2, T])
        ftile = sb("ftile", [1, NT, E1])
        ftf = sb("ftf", [1, NT])
        fti = sb("fti", [1, NT], I32)
        slot_tmp = sb("slot_tmp", [P, NT])
        sif = sb("sif", [P, NT])
        sidx1 = sb("sidx1", [P, NT], I32)
        gidx1 = sb("gidx1", [P, NT], I32)
        gcur = sb("gcur", [P, 4], I32)
        scur = sb("scur", [P, 4], I32)

        lst = sb("lst", [P, E0, 32])
        lstf = sb("lstf", [P, 32])
        lsti = sb("lsti", [P, 32], I32)
        idx = sb("idx", [P, E0, 4], I32)
        mrow = sb("mrow", [1, 2, P])
        wst = sb("wst", [P, 8, E0])
        gidx = sb("gidx", [P, 4], I32)
        sidx = sb("sidx", [P, 4], I32)
        pgate = sb("pgate", [P, 16])
        xg = small(0, 544).rearrange("p (k n) -> p k n", k=4)
        xgT = small(544, 256).rearrange("p (k n) -> p k n", k=2)
        w13 = sb("w13", [P, E0, 2 * H0])
        wd = w13[:].rearrange("p e (h n) -> p e h n", h=4)
        w2 = sb("w2", [P, E0, 2, D])
        sg = small(800, 512).rearrange("p (k n) -> p k n", k=2)
        gg = small(1312, 512).rearrange("p (k n) -> p k n", k=2)
        gT = small(1824, 512).rearrange("p (k n) -> p k n", k=2)
        we = sb("we", [P, 4])
        wk = sb("wk", [P, 4])
        yw = small(2336, 512).rearrange("p (k n) -> p k n", k=4)
        acc = sb("acc", [P, 2, J, D])

        d_fvar = sem("d_f_var")
        d_frstd = sem("d_f_rstd")
        d_acc0 = sem("d_acc0")
        d_acc1 = sem("d_acc1")
        d_accfree = sem("d_accfree")
        d_xvar = sem("d_xvar")
        d_xrstd = sem("d_xrstd")
        d_xh = sem("d_xh")
        d_xtps = sem("d_xtps")
        d_xt = sem("d_xt")
        d_qkv = sem("d_qkv")
        d_kvb = sem("d_kvb")
        d_prod = sem("d_prod")
        d_accum = sem("d_accum")
        d_state = sem("d_state")
        d_statefree = sem("d_statefree")
        q_prod = sem("q_prod")
        q_tr = sem("q_tr")
        q_trps = sem("q_trps")
        q_num = sem("q_num")
        q_r = sem("q_r")
        q_t = sem("q_t")
        q_den = sem("q_den")
        q_o = sem("q_o")
        q_y = sem("q_y")
        q_yvar = sem("q_yvar")
        q_yrstd = sem("q_yrstd")
        q_nmr = sem("q_nmr")
        q_yn = sem("q_yn")
        q_xvar = sem("q_xvar")
        q_xrstd = sem("q_xrstd")
        q_row = sem("q_row")
        q_rowst = sem("q_rowst")
        q_rtps = sem("q_rtps")
        q_rt = sem("q_rt")
        q_lg = sem("q_lg")
        q_lgc = sem("q_lgc")
        r_both = sem("r_both")
        r_ps = sem("r_ps")
        r_one = sem("r_one")
        r_slot = sem("r_slot")
        r_idx = sem("r_idx")
        r_fti = sem("r_fti")
        f_x = [sw_sem(f"f_rows_gathered_{q}") for q in range(4)]
        f_xtps = sem("f_xtps")
        f_xt = sem("f_xt")
        f_gu = sem("f_gu")
        f_silu = sem("f_silu")
        f_g = sem("f_g")
        f_gtps = sem("f_gtps")
        f_gt = sem("f_gt")
        f_y = sem("f_y")
        f_yr = sem("f_yr")
        f_st = [sw_sem(f"f_rows_stored_{q}") for q in range(4)]
        f_gcur = sem("f_gcur")
        f_scur = sem("f_scur")
        f_up = sem("f_up")
        q_st = sem("q_st")
        g_y0 = sem("g_y0")
        g_y1 = sem("g_y1")
        g_var = sem("g_var")
        g_rstd = sem("g_rstd")
        g_out = sem("g_out")
        g_st0 = sem("g_st0")
        g_st1 = sem("g_st1")
        r_w = sem("r_w")
        f_w = sem("f_w")
        d_z = sem("d_z")
        c_zero = sem("c_zero_filled")
        c_zst = sw_sem("c_sums_cleared")
        c_srch = sem("c_search_loaded")
        c_cnt = sem("c_count")
        c_tot = sem("c_total")
        c_post = sem("c_post_counts")
        c_postps = sem("c_post_sums")
        c_q = sem("c_slots")
        c_abps = sem("c_slots_by_token")
        c_one = sem("c_one_hots")
        c_lps = sem("c_list_in_psum")
        c_lst = sem("c_list")
        c_lstst = sem("c_list_stored")
        c_idx = sem("c_idx_loaded")
        c_mx = sem("c_max")
        c_mxps = sem("c_max_in_psum")
        c_ex = sem("c_exp")
        c_w = sem("c_weights_ready")
        c_gidx = sem("c_idx_copied")
        c_xg = [sw_sem(f"c_gathered_{k}") for k in range(4)]
        c_xtps = sem("c_xt_in_psum")
        c_xt = sem("c_xt")
        c_h = sem("c_h")
        c_sg = sem("c_silu")
        c_gg = sem("c_gated")
        c_gtps = sem("c_gt_in_psum")
        c_gt = sem("c_gt")
        c_y = sem("c_y")
        c_we = sem("c_slot_exp")
        c_wx = sem("c_slot_exp_done")
        c_yw = sem("c_yw")
        c_acc = sw_sem("c_added")
        c_added = sem("c_expert_added")
        f_stored = sem("f_pair_stored")
        c_accl = sem("c_sums_loaded")
        c_x2 = sem("c_x2")
        s_pch = sem("pool_chain")
        s_w1 = sem("ffn1_weights")
        s_w0 = sem("ffn0_weights")

        s_const = sem("const_loaded")
        s_alog = sem("alog_loaded")
        s_x = sem("x_loaded")
        s_fill = sem("constants_filled")
        s_dvech = sem("dve_chain")
        s_actch = sem("act_chain")
        s_wdt = sem("wdt_product")
        s_wa = sem("wa_ready")
        s_ea = sem("exp_alog")
        a_var = sem("a_var")
        a_rstd = sem("a_rstd")
        a_xn = sem("a_xn")
        a_xt_ps = sem("a_xt_in_psum")
        a_xt = sem("a_xt")
        a_proj = sem("a_proj")
        a_lz = sem("a_softplus_parts")
        a_dt = sem("a_dt")
        a_bar = sem("a_bar")
        a_dtv = sem("a_step_size")
        a_hc = sem("a_hc")
        a_y = sem("a_y")
        a_yvar = sem("a_y_var")
        a_yrstd = sem("a_y_rstd")
        a_ynmr = sem("a_y_shift")
        a_yn = sem("a_yn")
        a_x1var = sem("a_x1_var")
        a_x1rstd = sem("a_x1_rstd")
        a_x1n = sem("a_x1n")
        a_x1t_ps = sem("a_x1t_in_psum")
        a_x1t = sem("a_x1t")
        a_sc = sem("a_scores")
        a_row = sem("a_row_complete")
        a_st_ps = sem("a_score_rows_in_psum")
        a_st = sem("a_score_rows")
        a_rowst = sem("a_rows_stored")
        a_scst = sem("a_scores_stored")
        s_out = sem("out_stored")

        class Tile:

            def __init__(self, i, k):
                self.t, self.lap, self.ring, self.pair = 4 * i + k, i + k // 4, k % 4, k % 2

        def pipeline(eng, step, lead, lag, chain=None, per=0):
            def alone(s):
                if chain:
                    chain.begin(0, 0)
                step(lambda d: Tile(0, s + d) if 0 <= s + d < NT else None)
                if chain:
                    chain.end(1)
            for s in range(-lead, 8):
                alone(s)
            with eng.Fori(0, NT // 4 - 3) as i:
                if chain:
                    chain.begin(i, 4 * per)
                for k in range(8, 12):
                    step(lambda d: Tile(i, k + d))
                if chain:
                    chain.end(NT // 4 - 3)
            for s in range(NT - 4, NT + lag):
                alone(s)

        block = ctx.enter_context(nc.Block())
        x_d = inp["x"].rearrange("(b c j p) d -> c p b j d", b=NB, c=CH, j=J, p=P)
        row_d = x1row_dram.rearrange("(b c j p) d -> c b p j d", b=NB, c=CH, j=J, p=P)
        sum_d = sum_dram.rearrange("(b c j p) d -> c p b j d", b=NB, c=CH, j=J, p=P)
        sc_d = score_dram.rearrange("e (b c w) -> c e b w", b=NB, c=CH)
        Xv = X[:, :, :, :].rearrange("p b c (j d) -> p c b j d", j=J)

        @block.sync
        def _(sp):
            tiles = dict(wqkv=wqkv, gamma=gamma, wo=wo, wr=wr, tri128=tri128, iota_t=iota_t,
                         slot_pad=slot_pad, choice128=choice128, rev8=rev8, wa=wa, wxp=wxp, wdt=wdt, bdt=bdt, negA=negA, wout=wout, dp=dp, ident=ident, wg0=wg0, blk=blk,
                         tri=tri, bits=bits, iota=iota, pcol=pcol, tile128=tile128, emask=emask)
            for dst, name in CON:
                sp.dma_start(tiles[dst][:], inp[name]).then_inc(s_const, 16)
            with sp.Fori(0, CH) as c:
                sp.wait_ge(s_x, LEAD + c * 32)
                for b in range(NB):
                    sp.dma_start(Xv[:, ds(c, 1), b].rearrange("p o j d -> p (o j) d"),
                                 x_d[ds(c, 1), :, b].rearrange("o p j d -> (o p) j d")).then_inc(s_x, 16)
            with sp.Fori(0, CH) as c:
                for b in range(NB):
                    sp.wait_ge(a_row, LEAD + c * 2 + b + 1)
                    sp.dma_start(row_d[ds(c, 1), b].rearrange("o p j d -> (o p) j d"), row[:, b]).then_inc(a_rowst, 16)
                sp.wait_ge(a_st, LEAD + c * 2 + 2)
                sp.dma_start(sc_d[ds(c, 1)].rearrange("o e b w -> (o e) b w"), sT[:]).then_inc(a_scst, 16)
            sp.wait_ge(a_rowst, LEAD + 32 * CH)
            sp.wait_ge(a_scst, LEAD + 16 * CH)
            sp.dma_start(srch[:], score_dram.rearrange("e (s w) -> (e s) w", w=SEG)).then_inc(c_srch, 16)
            sp.dma_start(wgu[:], inp["wgu"]).then_inc(s_w1, 16)
            sp.dma_start(w13[:], inp["w13"]).then_inc(s_w0, 16)
            sp.dma_start(w2[:], inp["w2"]).then_inc(s_w0, 16)
            sp.wait_ge(c_lst, LEAD + 1)
            sp.dma_start(list_dram.rearrange("(p b) -> p b", b=32), lsti[:]).then_inc(c_lstst, 16)
            sp.wait_ge(c_lstst, LEAD + 16)
            sp.dma_start(idx[:], list_dram.rearrange("(e q k) -> q e k", e=E0, k=4)).then_inc(c_idx, 16)
            sp.wait_ge(c_acc, 16 * 4 * E0)
            sp.dma_start(wd, inp["wd"]).then_inc(s_w1, 16)
            sum_l = sum_dram.rearrange("(g j p) d -> g p j d", j=J, p=P)
            for b in range(NB):
                with sp.Fori(0, CH // 2) as i:
                    for u in range(2):
                        sp.wait_ge(d_accfree, LEAD + i * 2 + (b * 4 + u))
                        sp.dma_start(acc[:, u], sum_l[ds(2 * i + (4 * b + u), 1)].rearrange("o p j d -> (o p) j d")).then_inc(
                            (d_acc0, d_acc1)[u], 16)
                with sp.Fori(0, CH) as i:
                    sp.wait_ge(q_row, LEAD + i + (4 * b + 1))
                    sp.dma_start(x3row_dram.rearrange("(g j p) d -> g p j d", j=J, p=P)[ds(i + 4 * b, 1)]
                                 .rearrange("o p j d -> (o p) j d"), row[:, 0, :, 0:D]).then_inc(q_rowst, 16)
            for q in range(4):
                sp.wait_ge(f_st[q], 16 * (NT // 4))
            y_l = y_dram[0:2 * T * P, :].rearrange("(c g j p) d -> g p c j d", c=2, j=J, p=P)
            out_l = outs[0].rearrange("(g j p) d -> g p j d", j=J, p=P)
            x_l = X[:].rearrange("p b c (j d) -> p (b c) j d", j=J)
            with sp.Fori(0, NB * CH // 2) as i:
                for u in range(2):
                    sp.wait_ge(g_out, LEAD + 2 * i)
                    for c in range(2):
                        sp.dma_start(fin[:, u, c], y_l[ds(2 * i + u, 1), :, c].rearrange("o p j d -> (o p) j d")).then_inc(
                            (g_y0, g_y1)[u], 16)
                for u in range(2):
                    sp.wait_ge(g_out, LEAD + 2 * i + (u + 1))
                    sp.dma_start(out_l[ds(2 * i + u, 1)].rearrange("o p j d -> (o p) j d"),
                                 x_l[:, ds(2 * i + u, 1)].rearrange("p o j d -> p (o j) d")).then_inc(s_out, 16)
            sp.wait_ge(s_out, LEAD + 16 * NB * CH)

        @block.gpsimd
        def _(pool):
            nc.gpsimd.memset(mhalf[:], -0.5)
            nc.gpsimd.memset(ones[:], 1.0)
            nc.gpsimd.memset(carry[:], 0.0).then_inc(s_fill, 1)
            pool.wait_ge(s_fill, LEAD + 1)
            nc.gpsimd.memset(onesW[:], 1.0)
            nc.gpsimd.memset(zero[:], 0.0).then_inc(c_zero, 1)
            pool.wait_ge(c_zero, LEAD + 1)
            for t in range(T // 4):
                pool.dma_start(sum_dram.rearrange("(t k p) d -> t p k d", p=P, k=4)[t], zero[:]).then_inc(c_zst, 16)
            with pool.Fori(0, CH) as c:
                for b in range(NB):
                    pool.wait_ge(a_var, LEAD + c * 2 + b + 1)
                    nc.gpsimd.tensor_tensor(rstd[:, b], ve[:, b], mhalf[:, 0:J], ALU.pow).then_inc(a_rstd, 1)
                for b in range(NB):
                    pool.wait_ge(a_yvar, LEAD + c * 2 + b + 1)
                    nc.gpsimd.tensor_tensor(rstd[:, b], ve[:, b], mhalf[:, 0:J], ALU.pow).then_inc(a_yrstd, 1)
                for b in range(NB):
                    pool.wait_ge(a_x1var, LEAD + c * 2 + b + 1)
                    nc.gpsimd.tensor_tensor(rstd[:, b], ve[:, b], mhalf[:, 0:J], ALU.pow).then_inc(a_x1rstd, 1)
            pool.wait_ge(c_idx, LEAD + 16)
            pool.wait_ge(c_zst, 16 * T // 4)
            pc = Tally(pool, s_pch)

            def pool_gate(n):
                pc.wait()
                pc.mark(nc.gpsimd.tensor_tensor(pgate[:, n:n + 1], ones[:, 0:1], ones[:, 0:1], ALU.add))

            with pool.Fori(0, E0) as e:
                pc.begin(e, 9)
                pc.wait()
                pc.mark(nc.gpsimd.tensor_copy(gidx[:], idx[:, ds(e, 1), :].rearrange("p o k -> p (o k)")))
                for k in range(4):
                    pool.wait_ge(c_xtps, LEAD + e * 4 + k)
                    pool.wait_ge(c_we, LEAD + e * 4 + k)
                    pool_gate(k)
                    nc.gpsimd.indirect_dma_start(xg[:, k], None, x1row_dram,
                                                 bass.IndirectOffsetOnAxis(ap=gidx[:, k:k + 1].bitcast(U32), axis=0)).then_inc(c_xg[k], 16)
                for k in range(4):
                    pool.wait_ge(c_yw, LEAD + e * 4 + k + 1)
                    pool_gate(5 + k)
                    nc.gpsimd.indirect_dma_start(sum_dram, bass.IndirectOffsetOnAxis(ap=gidx[:, k:k + 1].bitcast(U32), axis=0), yw[:, k],
                                                 None, compute_op=ALU.add).then_inc(c_acc, 16)
                pool.wait_ge(c_acc, e * 64 + 64)
                pool.sem_inc(c_added, 1)
                pc.end(E0)
            def power(u, wait, n, done, count=J):
                pool.wait_ge(wait, LEAD + n)
                nc.gpsimd.tensor_tensor(rstd[:, u], ve[:, u], mhalf[:, 0:J], ALU.pow).then_inc(done, 1)
            for b in range(NB):
                with pool.Fori(0, CH // 2) as i:
                    for u in range(2):
                        n = 2 * i + (4 * b + u + 1)
                        power(u, d_fvar, n, d_frstd)
                        power(u, d_xvar, n, d_xrstd)
                with pool.Fori(0, CH) as i:
                    power(0, q_yvar, i + (4 * b + 1), q_yrstd)
                    power(0, q_xvar, i + (4 * b + 1), q_xrstd)
            pool.wait_ge(r_idx, LEAD + 1)
            pool.wait_ge(q_rowst, LEAD + 16 * NB * CH)
            def route(at):
                n = at(3)
                if n:
                    if not (isinstance(n.t, int) and n.t < 4):
                        pool.wait_ge(f_xtps, LEAD + n.t - 3)
                    pc.wait()
                    pc.mark(nc.gpsimd.tensor_copy(gcur[:, n.ring:n.ring + 1], gidx1[:, ds(n.t, 1)]))
                    pool_gate(0)
                    nc.gpsimd.indirect_dma_start(xr[:, n.ring], None, x3row_dram,
                                                 bass.IndirectOffsetOnAxis(ap=gcur[:, n.ring:n.ring + 1].bitcast(U32), axis=0)
                                                 ).then_inc(f_x[n.ring], 16)
                o = at(-3)
                if o:
                    pc.wait()
                    pool.wait_ge(f_yr, LEAD + o.t + 1)
                    pc.mark(nc.gpsimd.tensor_copy(scur[:, o.ring:o.ring + 1], sidx1[:, ds(o.t, 1)]))
                    pool_gate(1)
                    nc.gpsimd.indirect_dma_start(y_dram, bass.IndirectOffsetOnAxis(ap=scur[:, o.ring:o.ring + 1].bitcast(U32),
                                                                                   axis=0),
                                                 yr[:, o.ring], None).then_inc(f_st[o.ring], 16)
            pipeline(pool, route, 3, 3, pc, 4)
            with pool.Fori(0, NB * CH // 2) as i:
                for u in range(2):
                    power(u, g_var, 2 * i + (u + 1), g_rstd)

        @block.scalar
        def _(act):
            ch = Tally(act, s_actch)
            act.wait_ge(s_alog, LEAD + 1)
            nc.scalar.activation(negA[:], negA[:], ACT.Exp).then_inc(s_ea, 1)
            act.wait_ge(s_fill, LEAD + 1)
            with act.Fori(0, CH) as c:
                ch.begin(c, 2)
                for b in range(NB):
                    act.wait_ge(a_xt_ps, LEAD + c * 2 + b + 1)
                    nc.scalar.activation(xnT[:, b], bank[b][:], ACT.Copy).then_inc(a_xt, 1)
                act.wait_ge(a_proj, LEAD + c + 1)
                z = bank[2][0:32, :]
                ch.mark(nc.scalar.activation(az[:], z, ACT.Abs, bias=bdt[:, 0:1]))
                nc.scalar.activation(rz[:], z, ACT.Relu, bias=bdt[:, 0:1])
                ch.wait()
                ch.mark(nc.scalar.activation(ez[:], az[:], ACT.Exp, scale=-1.0))
                ch.wait()
                nc.scalar.activation(lz[:], ez[:], ACT.Ln, bias=ones[0:32, 0:1]).then_inc(a_lz, 1)
                act.wait_ge(a_dt, LEAD + c + 1)
                nc.scalar.activation(abar[:], dz[:], ACT.Exp).then_inc(a_bar, 1)
                for b in range(NB):
                    act.wait_ge(a_ynmr, LEAD + c * 2 + b + 1)
                    for j in range(J):
                        last = nc.scalar.activation(yn[:, b, j], bank[3 + b][:, j * P:(j + 1) * P], ACT.Identity,
                                                    bias=nmr[:, b, j:j + 1], scale=rstd[:, b, j:j + 1])
                    last.then_inc(a_yn, 1)
                for b in range(NB):
                    act.wait_ge(a_x1t_ps, LEAD + c * 2 + b + 1)
                    nc.scalar.activation(x1T[:, b], bank[5 + b][:], ACT.Copy).then_inc(a_x1t, 1)
                for b in range(NB):
                    act.wait_ge(a_st_ps, LEAD + c * 2 + b + 1)
                    act.wait_ge(a_scst, LEAD + 16 * c)
                    nc.scalar.activation(sT[:, b], bank[b][0:E0, :], ACT.Copy).then_inc(a_st, 1)
                ch.end(CH)
            act.wait_ge(c_mxps, LEAD + 2)
            nc.scalar.activation(base[:, 2:3], bank[4][:, 0:1], ACT.Copy, scale=-1.0).then_inc(c_ex, 1)
            act.wait_ge(c_ex, LEAD + 1)
            nc.scalar.activation(hit[:], srch[:], ACT.Exp, bias=base[:, 2:3]).then_inc(c_ex, 1)
            with act.Fori(0, E0) as e:
                for k in range(4):
                    act.wait_ge(c_xtps, LEAD + e * 4 + k + 1)
                    nc.scalar.activation(xgT[:, k % 2], bank[k % 2][:, 0:P], ACT.Copy).then_inc(c_xt, 1)
                    act.wait_ge(c_we, LEAD + e * 4 + k + 1)
                    nc.scalar.activation(we[:, k:k + 1], wk[:, k:k + 1], ACT.Exp).then_inc(c_wx, 1)
                    act.wait_ge(c_h, LEAD + e * 4 + k + 1)
                    nc.scalar.activation(sg[:, k % 2], bank[2 + k % 2][:, 0:H0], ACT.Silu).then_inc(c_sg, 1)
                    act.wait_ge(c_gtps, LEAD + e * 4 + k + 1)
                    nc.scalar.activation(gT[:, k % 2], bank[4 + k % 2][:, 0:H0], ACT.Copy).then_inc(c_gt, 1)

            for b in range(NB):
                with act.Fori(0, CH // 2) as i:
                    for u in range(2):
                        n = 2 * i + (4 * b + u)
                        act.wait_ge(d_xtps, LEAD + n + 1)
                        nc.scalar.activation(xnT[:, u], bank[0][:], ACT.Copy).then_inc(d_xt, 1)
                        for j in range(J):
                            act.wait_ge(d_qkv, LEAD + n * 4 + (j + 1))
                            if j >= 2:
                                act.wait_ge(d_accum, LEAD + n * 4 + (j - 1))
                            else:
                                act.wait_ge(d_accum, LEAD + n * 4)
                            nc.scalar.activation(kvb[:, j % 2, 1:], bank[1 + j % 2][:, 0:320], ACT.Copy)
                            nc.scalar.activation(kc[:, j % 2].rearrange("p (h i) -> p h i", h=HD), bank[1 + j % 2][:, D:320]
                                                 .rearrange("p (h i) -> p h i", h=HD)[:, :, 0:DH], ACT.Copy)
                            nc.scalar.activation(q_all[:, ds(n * 4 + j, 1)].rearrange("p o n -> p (o n)"),
                                                 bank[1 + j % 2][:, 320:], ACT.Copy).then_inc(d_kvb, 1)
                with act.Fori(0, CH) as i:
                    n = i + 4 * b
                    for j in range(J):
                        m = n * 4 + j
                        for h, w in enumerate((512, 512, 256)):
                            act.wait_ge(q_trps, LEAD + m * 3 + (h + 1))
                            if h == 0:
                                act.wait_ge(q_num, LEAD + n * 4 + max(j - 1, 0))
                            last = nc.scalar.activation(prodT[:, j % 2, 512 * h:512 * h + w], bank[h][:, 0:w], ACT.Copy)
                            last.then_inc(q_tr, 1)
                        nc.scalar.activation(qTg[:, j * P:(j + 1) * P], bank[2][:, P:2 * P], ACT.Copy).then_inc(q_tr, 1)
                    act.wait_ge(q_nmr, LEAD + n + 1)
                    for j in range(J):
                        last = nc.scalar.activation(yn[:, 0, j], bank[6][:, j * P:(j + 1) * P], ACT.Identity,
                                                    bias=nmr[:, 0, j:j + 1], scale=rstd[:, 0, j:j + 1])
                    last.then_inc(q_yn, 1)
                    act.wait_ge(q_rtps, LEAD + n + 1)
                    nc.scalar.activation(x1T[:, 0], bank[7][:], ACT.Copy).then_inc(q_rt, 1)
            act.wait_ge(r_w, LEAD + 1)
            nc.scalar.activation(top[:, 1], top[:, 1], ACT.Exp).then_inc(f_w, 1)
            def move(at):
                n, m, o = at(1), at(0), at(-1)
                if n:
                    act.wait_ge(f_xtps, LEAD + n.t + 1)
                    if not (isinstance(n.t, int) and n.t < 2):
                        act.wait_ge(f_up, LEAD + n.t - 1)
                    nc.scalar.activation(xrT[:, n.pair], bank[(0, 7)[n.pair]][:, 0:D], ACT.Copy).then_inc(f_xt, 1)
                if m:
                    act.wait_ge(f_gu, LEAD + m.t + 1)
                    nc.scalar.activation(sgl[:, m.pair], bank[1 + m.pair][:], ACT.Silu).then_inc(f_silu, 1)
                if o:
                    act.wait_ge(f_gtps, LEAD + o.t + 1)
                    if not (isinstance(o.t, int) and o.t < 2):
                        act.wait_ge(f_y, LEAD + o.t - 1)
                    nc.scalar.activation(glT[:, o.pair], bank[5][:], ACT.Copy).then_inc(f_gt, 1)
            pipeline(act, move, 1, 1)

        @block.vector
        def _(dve):
            ch = Tally(dve, s_dvech)
            dve.wait_ge(s_const, LEAD + NC)
            nc.vector.tensor_scalar(negA[:], negA[:], 85.0, None, ALU.min).then_inc(s_alog, 1)
            nc.vector.tensor_scalar(diagD[:], ident[:], dp[:, 0:1], None, ALU.mult)
            nc.vector.tensor_copy(bitsf[:], bits[:])
            dve.wait_ge(s_ea, LEAD + 1)
            nc.vector.tensor_scalar(negA[:], negA[:], -1.0, None, ALU.mult)
            dve.wait_ge(s_wdt, LEAD + 1)
            nc.vector.tensor_copy(wa[:, 0, 0:NS], bank[7][:, 0:NS])
            nc.vector.tensor_copy(wa[:, 1, NS:2 * NS], bank[7][:, 0:NS]).then_inc(s_wa, 1)

            def stats(src, b, c, ready):
                nc.vector.memset(gate[:], 0.0)
                for j in range(J):
                    last = nc.vector.bn_stats(st[:, b, j], src(b, j))
                ch.mark(last)
                ch.wait()
                nc.vector.memset(gate[:], 0.0)
                for j in range(J):
                    last = nc.vector.bn_aggr(mv[:, b, j], st[:, b, j])
                ch.mark(last)
                ch.wait()
                nc.vector.tensor_scalar(ve[:, b], mv[:, b, :, 1], EPS, None, ALU.add).then_inc(ready, 1)

            with dve.Fori(0, CH) as c:
                ch.begin(c, 20)
                def xt(b, j):
                    return Xv[:, ds(c, 1), b, j].rearrange("p o d -> p (o d)")
                dve.wait_ge(s_x, LEAD + 32 * (c + 1))
                for b in range(NB):
                    stats(xt, b, c, a_var)
                dve.wait_ge(a_xt_ps, LEAD + c * 2)
                for b in range(NB):
                    dve.wait_ge(a_rstd, LEAD + c * 2 + b + 1)
                    for j in range(J):
                        last = nc.vector.tensor_scalar(xn[:, b, j], xt(b, j), mv[:, b, j, 0:1], rstd[:, b, j:j + 1],
                                                       ALU.subtract, ALU.mult)
                    last.then_inc(a_xn, 1)
                PJ = bank[2]
                dve.wait_ge(a_lz, LEAD + c + 1)
                ch.mark(nc.vector.tensor_scalar(dz[:], ez[:], 1.0, 1.0, ALU.add, ALU.subtract))
                ch.wait()
                ch.mark(nc.vector.tensor_tensor(dz[:], ez[:], dz[:], ALU.subtract))
                ch.wait()
                ch.mark(nc.vector.tensor_tensor(dz[:], dz[:], lz[:], ALU.add))
                ch.wait()
                nc.vector.tensor_tensor(dtt[:], dz[:], rz[:], ALU.add).then_inc(a_dtv, 1)
                dve.wait_ge(a_dtv, LEAD + c + 1)
                nc.vector.tensor_scalar(dz[:], dtt[:], negA[:, 0:1], -200.0, ALU.mult, ALU.max).then_inc(a_dt, 1)
                ch.mark(nc.vector.tensor_tensor(bx[:], dtt[:], PJ[32:64, :], ALU.mult))
                ch.wait()
                ch.mark(nc.vector.tensor_tensor(bx[:], bx[:], PJ[96:128, :], ALU.mult))
                ch.wait()
                dve.wait_ge(a_bar, LEAD + c + 1)
                ch.mark(nc.vector.tensor_tensor_scan(hh[:], abar[:], bx[:], carry[:, 0:1], ALU.mult, ALU.add))
                ch.wait()
                nc.vector.tensor_copy(carry[:], hh[:, W - 1:W])
                nc.vector.tensor_tensor(hc[:], hh[:], PJ[64:96, :], ALU.mult).then_inc(a_hc, 1)
                for b in range(NB):
                    dve.wait_ge(a_y, LEAD + c * 2 + b + 1)
                    stats(lambda b, j: bank[3 + b][:, j * P:(j + 1) * P], b, c, a_yvar)
                for b in range(NB):
                    dve.wait_ge(a_yrstd, LEAD + c * 2 + b + 1)
                    nc.vector.scalar_tensor_tensor(nmr[:, b], mv[:, b, :, 0], -1.0, rstd[:, b], ALU.mult,
                                                   ALU.mult).then_inc(a_ynmr, 1)
                for b in range(NB):
                    dve.wait_ge(a_yn, LEAD + c * 2 + b + 1)
                    xc = Xv[:, ds(c, 1), b].rearrange("p o j d -> p (o j) d")
                    ch.mark(nc.vector.tensor_tensor(xc, xc, yn[:, b], ALU.add))
                    ch.wait()
                    stats(xt, b, c, a_x1var)
                for b in range(NB):
                    dve.wait_ge(a_x1rstd, LEAD + c * 2 + b + 1)
                    dve.wait_ge(a_rowst, LEAD + c * 32)
                    for j in range(J):
                        last = nc.vector.tensor_scalar(row[:, b, j, 0:D], xt(b, j), mv[:, b, j, 0:1],
                                                       rstd[:, b, j:j + 1], ALU.subtract, ALU.mult)
                    last.then_inc(a_x1n, 1)
                for b in range(NB):
                    dve.wait_ge(a_sc, LEAD + c * 2 + 2)
                    nc.vector.tensor_copy(row[:, b, :, D:ROWS], bank[7][:, 64 * b:64 * b + J * E0]
                                          .rearrange("p (j e) -> p j e", j=J)).then_inc(a_row, 1)
                ch.end(CH)

            def count(out):
                return nc.vector.tensor_scalar(hit[:], srch[:], cand[:].bitcast(F32), None, ALU.is_ge, ALU.add,
                                               accum_out=out)
            ch.begin(0, 2)
            ch.mark(nc.vector.memset(cand[:], 0))
            ch.wait()
            dve.wait_ge(c_srch, LEAD + 16)
            count(cntb[:]).then_inc(c_cnt, 1)
            dve.wait_ge(c_tot, LEAD + 1)
            ch.mark(nc.vector.tensor_scalar(cand[:].bitcast(I32), bank[7][:, 0:1], float(CAP), -1.0, ALU.is_lt, ALU.mult))
            ch.wait()
            ch.end(1)
            ch.begin(0, 1)
            ch.mark(nc.vector.tensor_tensor(cand[:], cand[:], bits[:, 0:1], ALU.bitwise_xor))
            ch.wait()
            ch.end(1)
            with dve.Fori(0, 31) as i:
                ch.begin(i, 2)
                count(cntb[:]).then_inc(c_cnt, 1)
                dve.wait_ge(c_tot, LEAD + i + 2)
                ch.mark(nc.vector.scalar_tensor_tensor(step[:], bank[7][:, 0:1], float(CAP), bitsf[:, ds(i, 1)],
                                                       ALU.is_lt, ALU.mult))
                ch.wait()
                ch.mark(nc.vector.scalar_tensor_tensor(cand[:], cand[:], bits[:, ds(i + 1, 1)], step[:],
                                                       ALU.bitwise_xor, ALU.bitwise_xor))
                ch.wait()
                ch.end(31)
            ch.begin(0, 24)
            thr = cand[:].bitcast(F32)
            nc.vector.tensor_scalar(sel[:], srch[:], thr, None, ALU.is_gt, ALU.add, accum_out=cg[:, 0:1])
            ch.mark(nc.vector.tensor_reduce(cg[:, 3:4], srch[:], AX.X, ALU.max))
            nc.vector.tensor_scalar(eq[:], srch[:], thr, None, ALU.is_equal, ALU.add,
                                    accum_out=cg[:, 1:2]).then_inc(c_post, 1)
            dve.wait_ge(c_postps, LEAD + 1)
            nc.vector.tensor_scalar(base[:, 0:1], bank[6][:, 0:1], -1.0, float(CAP), ALU.mult, ALU.add)
            ch.mark(nc.vector.tensor_copy(base[:, 1:2], bank[6][:, 1:2]))
            ch.wait()
            ch.mark(nc.vector.tensor_tensor_scan(rank[:], onesW[:], eq[:], base[:, 1:2], ALU.mult, ALU.add))
            ch.wait()
            ch.mark(nc.vector.scalar_tensor_tensor(rank[:], rank[:], base[:, 0:1], eq[:], ALU.is_le, ALU.mult))
            ch.wait()
            ch.mark(nc.vector.tensor_tensor(sel[:], sel[:], rank[:], ALU.add))
            ch.wait()
            nc.vector.tensor_reduce(cg[:, 2:3], sel[:], AX.X, ALU.add).then_inc(c_post, 1)
            dve.wait_ge(c_postps, LEAD + 2)
            ch.mark(nc.vector.tensor_copy(base[:, 3:4], bank[6][:, 2:3]))
            ch.wait()
            ch.mark(nc.vector.tensor_tensor_scan(rank[:], onesW[:], sel[:], base[:, 3:4], ALU.mult, ALU.add))
            ch.wait()
            ch.mark(nc.vector.tensor_tensor(rank[:], rank[:], sel[:], ALU.mult))
            ch.wait()
            ch.mark(nc.vector.tensor_scalar(qi[:, 0], rank[:], -1.0, None, ALU.add))
            ch.wait()
            ch.mark(nc.vector.tensor_scalar(qi[:, 1], qi[:, 0], 31, None, ALU.bitwise_and))
            ch.wait()
            ch.mark(nc.vector.tensor_scalar(qi[:, 0], qi[:, 0], 5, None, ALU.arith_shift_right))
            ch.wait()
            nc.vector.tensor_copy(qf[:], qi[:]).then_inc(c_q, 1)
            dve.wait_ge(c_mxps, LEAD + 1)
            ch.mark(nc.vector.tensor_reduce(mrow[:, 0, 0:E0], bank[3][0:1, 0:P].rearrange("p (e s) -> p e s", e=E0), AX.X,
                                            ALU.max))
            ch.wait()
            nc.vector.tensor_copy(mrow[:, 1].rearrange("p (e s) -> p e s", e=E0),
                                  mrow[:, 0, 0:E0].unsqueeze(2).to_broadcast([1, E0, 16])).then_inc(c_mx, 1)
            dve.wait_ge(c_mxps, LEAD + 2)
            dve.wait_ge(c_ex, LEAD + 2)
            nc.vector.tensor_scalar(wst[:, 0], bank[5][:, 0:E0], -1.0, None, ALU.mult)
            ch.mark(nc.vector.tensor_tensor(hit[:], hit[:], sel[:], ALU.mult))
            ch.wait()
            ch.mark(nc.vector.tensor_reduce(cg[:, 0:1], hit[:], AX.X, ALU.add))
            ch.wait()
            nc.vector.tensor_scalar(wst[:, 1], emask[:], cg[:, 0:1], None, ALU.mult).then_inc(c_mx, 1)
            dve.wait_ge(c_abps, LEAD + 1)
            abT = bank[2][:].rearrange("p (w h q) -> p w h q", w=2, h=2)
            for w, n, one in ((0, 16, oneA), (1, 32, oneB)):
                for e in range(E0):
                    last = nc.vector.tensor_tensor(
                        one[:].rearrange("p (s h) e n -> p h s e n", h=2)[:, :, :, e],
                        abT[:, w, :, 16 * e:16 * e + 16].unsqueeze(3).to_broadcast([P, 2, 16, n]),
                        iota[:, 0:n].unsqueeze(1).unsqueeze(1).to_broadcast([P, 2, 16, n]), ALU.is_equal)
            ch.mark(last)
            ch.wait()
            nc.vector.tensor_scalar(valP[:], oneB[:], pcol[:, 0:1], None, ALU.mult)
            nc.vector.tensor_tensor(valT[:].rearrange("p t e n -> p t (e n)"), oneB[:].rearrange("p t e n -> p t (e n)"),
                                    tile128[:].unsqueeze(2).to_broadcast([P, T, 256]), ALU.mult).then_inc(c_one, 1)
            dve.wait_ge(c_lps, LEAD + 1)
            ch.mark(nc.vector.tensor_tensor(lst[:], bank[1][:, 0:256].rearrange("p (e n) -> p e n", e=E0),
                                            emask[:].unsqueeze(2).to_broadcast([P, E0, 32]), ALU.mult))
            ch.wait()
            ch.mark(nc.vector.tensor_reduce(lstf[:], lst[:].rearrange("p e n -> p n e"), AX.X, ALU.add))
            ch.wait()
            nc.vector.tensor_copy(lsti[:], lstf[:]).then_inc(c_lst, 1)
            dve.wait_ge(c_mxps, LEAD + 3)
            ch.mark(nc.vector.reciprocal(wst[:, 2], bank[6][:, 8:16]))
            ch.wait()
            ch.end(1)

            with dve.Fori(0, E0) as e:
                ch.begin(e, 4)
                for k in range(4):
                    dve.wait_ge(c_xg[k], e * 16 + 16)
                    nc.vector.tensor_tensor(wk[:, k:k + 1], xg[:, k, ds(e + D, 1)], wst[:, 0, ds(e, 1)],
                                            ALU.add).then_inc(c_we, 1)
                    dve.wait_ge(c_sg, LEAD + e * 4 + k + 1)
                    nc.vector.tensor_tensor(gg[:, k % 2], sg[:, k % 2], bank[2 + k % 2][:, H0:], ALU.mult).then_inc(c_gg, 1)
                    dve.wait_ge(c_wx, LEAD + e * 4 + k + 1)
                    ch.mark(nc.vector.tensor_scalar(wk[:, k:k + 1], we[:, k:k + 1], wst[:, 2, ds(e, 1)], None, ALU.mult))
                    ch.wait()
                    dve.wait_ge(c_y, LEAD + e * 4 + k + 1)
                    dve.wait_ge(c_added, LEAD + e)
                    nc.vector.tensor_scalar(yw[:, k], bank[6 + k % 2][:, 0:D], wk[:, k:k + 1], None, ALU.mult).then_inc(c_yw, 1)
                ch.end(E0)
            def stats1(src, u, ready):
                nc.vector.memset(gate[:], 0.0)
                for j in range(J):
                    last = nc.vector.bn_stats(st[:, u, j], src(j))
                ch.mark(last)
                ch.wait()
                nc.vector.memset(gate[:], 0.0)
                for j in range(J):
                    last = nc.vector.bn_aggr(mv[:, u, j], st[:, u, j])
                ch.mark(last)
                ch.wait()
                last = nc.vector.tensor_scalar(ve[:, u], mv[:, u, :, 1], EPS, None, ALU.add)
                if ready is not None:
                    last.then_inc(ready, 1)
                else:
                    ch.mark(last)
                    ch.wait()

            def windows(base):
                part_ = list(base.ap)[0]
                first = bass.AP(tensor=base.tensor, offset=base.offset, ap=[part_, (0, ND), (KW, HD), (1, DH)])
                second = bass.AP(tensor=base.tensor, offset=base.offset, ap=[part_, (1, ND), (KW, HD), (1, DH)])
                return first, second

            xl = X[:].rearrange("p b c (j d) -> p (b c) j d", j=J)
            nc.vector.tensor_scalar(halfblk[:], blk[:], 0.5, None, ALU.mult)
            nc.vector.memset(kvb[:, :, 0:1], 1.0)
            nc.vector.memset(zerob[:], 0.0)
            nc.vector.tensor_copy(iota_b[:], iota_t[:])
            nc.vector.tensor_scalar(wqkv[:, 0:320], wqkv[:, 0:320], gamma[:, 0:1], None, ALU.mult)
            nc.vector.tensor_scalar(wqkv[:, 320:], wqkv[:, 320:], gamma[:, 0:1], float(DH) ** -0.5, ALU.mult,
                                    ALU.mult).then_inc(d_z, 1)
            for b in range(NB):
                with dve.Fori(0, CH // 2) as i:
                    ch.begin(i, 12)
                    for u in range(2):
                        n = 2 * i + (4 * b + u)
                        xs = lambda j: xl[:, ds(n, 1), j].rearrange("p o d -> p (o d)")
                        dve.wait_ge((d_acc0, d_acc1)[u], LEAD + 16 * i + (32 * b + 16))
                        stats1(lambda j: acc[:, u, j], u, d_fvar)
                        dve.wait_ge(d_frstd, LEAD + n + 1)
                        for j in range(J):
                            last = nc.vector.tensor_scalar(acc[:, u, j], acc[:, u, j], mv[:, u, j, 0:1],
                                                           rstd[:, u, j:j + 1], ALU.subtract, ALU.mult)
                        ch.mark(last)
                        ch.wait()
                        xc = xl[:, ds(n, 1)].rearrange("p o j d -> p (o j) d")
                        nc.vector.tensor_tensor(xc, xc, acc[:, u], ALU.add).then_inc(d_accfree, 1)
                        dve.wait_ge(d_accfree, LEAD + n + 1)
                        stats1(xs, u, None)
                        nc.vector.scalar_tensor_tensor(ve[:, u], ve[:, u], 1e-24 / D, mv[:, u, :, 1], ALU.mult,
                                                       ALU.max).then_inc(d_xvar, 1)
                        dve.wait_ge(d_xrstd, LEAD + n + 1)
                        for j in range(J):
                            last = nc.vector.tensor_scalar(xn[:, u, j], xs(j), mv[:, u, j, 0:1],
                                                           rstd[:, u, j:j + 1], ALU.subtract, ALU.mult)
                        last.then_inc(d_xh, 1)
                        for j in range(J):
                            dve.wait_ge(d_kvb, LEAD + n * 4 + (j + 1))
                            first, second = windows(kvb[:, j % 2, 1 + D:])
                            nc.vector.tensor_tensor(prod[:, j % 2].rearrange("p (d h i) -> p d h i", d=ND, h=HD),
                                                    first, second, ALU.mult).then_inc(d_prod, 1)
                    ch.end(CH // 2)
                dve.wait_ge(d_accum, LEAD + 16 * (b + 1))
                ch.begin(0, 5)
                hm = blk[:].unsqueeze(1)
                for k in range(2):
                    nc.vector.tensor_tensor(smat[:, 4 * k:4 * k + 4], bank[3 + k][:].rearrange("p (d n) -> p d n", d=4),
                                            hm.to_broadcast([P, 4, P]), ALU.mult)
                nc.vector.tensor_tensor(smat[:, 8], bank[5][:, 0:P], halfblk[:], ALU.mult)
                nc.vector.tensor_tensor(smat[:, 9], bank[5][:, P + 1:2 * P + 1], blk[:], ALU.mult)
                nc.vector.tensor_tensor(kk[:], bank[5][:, 2 * P + 1:3 * P + 1], blk[:], ALU.mult)
                nc.vector.tensor_scalar(sums[:, 0:1], bank[5][:, P:P + 1], 2.0, None, ALU.mult)
                ch.mark(nc.vector.tensor_copy(sums[:, 1:2], bank[5][:, 3 * P + 1:3 * P + 2]))
                ch.wait()
                nc.vector.tensor_scalar(smat[:, 0], smat[:, 0], 0.5, None, ALU.mult).then_inc(d_state, 1)
                ch.end(1)
                with dve.Fori(0, CH) as i:
                    ch.begin(i, 7)
                    n = i + 4 * b
                    for j in range(J):
                        dve.wait_ge(q_trps, LEAD + n * 12 + 3 * max(j - 1, 0))
                        nc.vector.tensor_copy(qst[:, j % 2].rearrange("p (h i) -> p h i", h=HD), q_all[:, ds(n * 4 + j, 1)]
                                              .rearrange("p o (h i) -> p (o h) i", h=HD)[:, :, 0:DH])
                        first, second = windows(q_all[:, ds(n * 4 + j, 1)].rearrange("p o n -> p (o n)"))
                        nc.vector.tensor_tensor(prod[:, j % 2].rearrange("p (d h i) -> p d h i", d=ND, h=HD),
                                                first, second, ALU.mult).then_inc(q_prod, 1)
                    dve.wait_ge(q_r, LEAD + n + 1)
                    nc.vector.scalar_tensor_tensor(dt_[:], bank[5][:], sums[:, 0:1], qTg[:], ALU.add,
                                                   ALU.mult).then_inc(q_t, 1)
                    dve.wait_ge(q_den, LEAD + n + 1)
                    ch.mark(nc.vector.tensor_scalar(rden[:], bank[5][:], float(L), 1e-5, ALU.add, ALU.max))
                    ch.wait()
                    ch.mark(nc.vector.reciprocal(rden[:], rden[:]))
                    ch.wait()
                    nc.vector.scalar_tensor_tensor(oT[:], bank[3][:], sums[:, 1:2], rden[:], ALU.add,
                                                   ALU.mult).then_inc(q_o, 1)
                    dve.wait_ge(q_y, LEAD + n + 1)
                    stats1(lambda j: bank[6][:, j * P:(j + 1) * P], 0, q_yvar)
                    dve.wait_ge(q_yrstd, LEAD + n + 1)
                    nc.vector.scalar_tensor_tensor(nmr[:, 0], mv[:, 0, :, 0], -1.0, rstd[:, 0], ALU.mult,
                                                   ALU.mult).then_inc(q_nmr, 1)
                    dve.wait_ge(q_yn, LEAD + n + 1)
                    xc = xl[:, ds(n, 1)].rearrange("p o j d -> p (o j) d")
                    ch.mark(nc.vector.tensor_tensor(xc, xc, yn[:, 0], ALU.add))
                    ch.wait()
                    xs = lambda j: xl[:, ds(n, 1), j].rearrange("p o d -> p (o d)")
                    stats1(xs, 0, q_xvar)
                    dve.wait_ge(q_xrstd, LEAD + n + 1)
                    dve.wait_ge(q_rowst, LEAD + n * 16)
                    for j in range(J):
                        last = nc.vector.tensor_scalar(row[:, 0, j, 0:D], xs(j), mv[:, 0, j, 0:1],
                                                       rstd[:, 0, j:j + 1], ALU.subtract, ALU.mult)
                    last.then_inc(q_row, 1)
                    dve.wait_ge(q_lg, LEAD + n + 1)
                    nc.vector.tensor_copy(lg[:, ds(n * 4, 4)], bank[7][:, 0:J * E1].rearrange("p (j e) -> p j e", j=J)).then_inc(
                        q_lgc, 1)
                    ch.end(CH)

            dve.wait_ge(q_lgc, LEAD + NB * CH)
            ch.begin(0, 0)

            def do(ins):
                ch.mark(ins)
                ch.wait()

            rv = rev8[:].unsqueeze(1).to_broadcast([P, T, E1])
            for c in range(2):
                do(nc.vector.tensor_reduce(top[:, c], lg[:], AX.X, ALU.max))
                do(nc.vector.tensor_tensor(tmp[:], lg[:], top[:, c].unsqueeze(2).to_broadcast([P, T, E1]), ALU.is_equal))
                do(nc.vector.tensor_tensor(tmp[:], tmp[:], rv, ALU.mult))
                do(nc.vector.tensor_reduce(slot[:, 0], tmp[:], AX.X, ALU.max))
                do(nc.vector.tensor_tensor(oh[:, c], rv, slot[:, 0].unsqueeze(2).to_broadcast([P, T, E1]), ALU.is_equal))
                if c == 0:
                    do(nc.vector.scalar_tensor_tensor(lg[:], oh[:, 0], -3e38, lg[:], ALU.mult, ALU.add))
            nc.vector.tensor_tensor(both[:].rearrange("p e t -> p t e"), oh[:, 0], oh[:, 1], ALU.add).then_inc(r_both, 1)
            nc.vector.tensor_tensor(top[:, 1], top[:, 1], top[:, 0], ALU.subtract).then_inc(r_w, 1)
            dve.wait_ge(r_ps, LEAD + 2)
            f2 = "p e t -> p (e t)"
            do(nc.vector.tensor_tensor_scan(scan[:].rearrange(f2), onesW[:], bank[2][:, 0:256], 0.0, ALU.mult, ALU.add))
            ends = scan[:, :, T - 1]
            nc.vector.memset(off[:, 0, 0:1], 0.0)
            do(nc.vector.tensor_copy(off[:, 0, 1:E1], ends[:, 0:E1 - 1]))
            do(nc.vector.tensor_tensor(off[:, 1], ends, off[:, 0], ALU.subtract))
            do(nc.vector.tensor_scalar(offi[:], off[:, 1], float(P - 1), None, ALU.add))
            do(nc.vector.tensor_scalar(offi[:], offi[:], 7, None, ALU.arith_shift_right))
            do(nc.vector.tensor_copy(off[:, 1], offi[:]))
            do(nc.vector.tensor_tensor_scan(off[:, 2], onesW[:, 0:E1], off[:, 1], 0.0, ALU.mult, ALU.add))
            do(nc.vector.tensor_tensor(off[:, 3], off[:, 2], off[:, 1], ALU.subtract))
            do(nc.vector.scalar_tensor_tensor(off[:, 3], off[:, 3], float(P), off[:, 0], ALU.mult, ALU.subtract))
            do(nc.vector.tensor_tensor(scan[:].rearrange(f2), scan[:].rearrange(f2), bank[2][:, 0:256], ALU.subtract))
            do(nc.vector.tensor_tensor(scan[:].rearrange(f2), scan[:].rearrange(f2), bank[1][:, 0:256], ALU.add))
            do(nc.vector.tensor_tensor(scan[:], scan[:], off[:, 3].unsqueeze(2).to_broadcast([P, E1, T]), ALU.add))
            for c in range(2):
                do(nc.vector.tensor_tensor(tmp[:], oh[:, c], scan[:].rearrange("p e t -> p t e"), ALU.mult))
                do(nc.vector.tensor_reduce(slot[:, c], tmp[:], AX.X, ALU.add))
            do(nc.vector.tensor_copy(sloti[:, 0], slot[:]))
            do(nc.vector.tensor_scalar(sloti[:, 1], sloti[:, 0], P - 1, None, ALU.bitwise_and))
            do(nc.vector.tensor_scalar(sloti[:, 0], sloti[:, 0], 7, None, ALU.arith_shift_right))
            do(nc.vector.tensor_copy(slotf[:], sloti[:]))
            nc.vector.tensor_scalar(val[:, 0], slotf[:, 1], -1.0, pcol[:, 0:1], ALU.mult, ALU.add)
            do(nc.vector.scalar_tensor_tensor(val[:, 1], slotf[:, 0], -float(P), choice128[:], ALU.mult, ALU.add))
            do(nc.vector.tensor_tensor(ftile[:], iota_t[0:1, 0:NT].unsqueeze(2).to_broadcast([1, NT, E1]),
                                       off[0:1, 2].unsqueeze(1).to_broadcast([1, NT, E1]), ALU.is_ge))
            do(nc.vector.tensor_reduce(ftf[:], ftile[:], AX.X, ALU.add))
            nc.vector.tensor_scalar(fti[:], ftf[:], float(E1 - 1), None, ALU.min).then_inc(r_fti, 1)
            ch.end(1)
            with dve.Fori(0, T) as t:
                for c in range(2):
                    v = oneV.rearrange("p (c a n) -> p c a n", c=2, a=2)[:, c]
                    dve.wait_ge(r_slot, LEAD + t * 2)
                    nc.vector.tensor_scalar(oneLo2[:, c],
                                            iota_b[:], slotf[:, 1, c, ds(t, 1)], None, ALU.is_equal)
                    nc.vector.tensor_scalar(v[:, 0], iota_b[:, 0:NT], slotf[:, 0, c, ds(t, 1)], val[:, 0, c, ds(t, 1)],
                                            ALU.is_equal, ALU.mult)
                    nc.vector.tensor_scalar(v[:, 1], iota_b[:, 0:NT], slotf[:, 0, c, ds(t, 1)],
                                            val[:, 1, c, ds(t, 1)], ALU.is_equal, ALU.mult).then_inc(r_one, 1)
            dve.wait_ge(r_slot, LEAD + 2 * T)
            ch.begin(0, 0)
            nc.vector.tensor_copy(slot_tmp[:], bank[3][:, NT:2 * NT])
            do(nc.vector.tensor_copy(sif[:], bank[3][:, 0:NT]))
            do(nc.vector.tensor_tensor(sif[:], sif[:], slot_tmp[:], ALU.add))
            do(nc.vector.tensor_tensor(sif[:], sif[:], slot_pad[:], ALU.add))
            do(nc.vector.tensor_copy(sidx1[:], sif[:]))
            nc.vector.tensor_scalar(gidx1[:], sidx1[:], T * P - 1, None, ALU.bitwise_and).then_inc(r_idx, 1)
            dve.wait_ge(f_w, LEAD + 1)
            do(nc.vector.tensor_scalar(wts[:, 0], top[:, 1], 1.0, None, ALU.add))
            do(nc.vector.reciprocal(wts[:, 0], wts[:, 0]))
            do(nc.vector.tensor_tensor(wts[:, 1], wts[:, 0], top[:, 1], ALU.mult))
            ch.end(1)
            def gated(at):
                m, o = at(0), at(-2)
                if m:
                    dve.wait_ge(f_silu, LEAD + m.t + 1)
                    dve.wait_ge(f_up, LEAD + m.t + 1)
                    if not (isinstance(m.t, int) and m.t < 2):
                        dve.wait_ge(f_gtps, LEAD + m.t - 1)
                    nc.vector.tensor_tensor(gl[:, m.pair], sgl[:, m.pair], bank[3 + m.pair][:], ALU.mult).then_inc(f_g, 1)
                if o:
                    dve.wait_ge(f_y, LEAD + o.t + 1)
                    if not (isinstance(o.t, int) and o.t < 4):
                        dve.wait_ge(f_st[o.ring], 16 * o.lap)
                    nc.vector.tensor_copy(yr[:, o.ring], bank[6][:, 0:D]).then_inc(f_yr, 1)
            pipeline(dve, gated, 0, 2)
            with dve.Fori(0, NB * CH // 2) as i:
                ch.begin(i, 10)
                for u in range(2):
                    n = 2 * i + u
                    dve.wait_ge((g_y0, g_y1)[u], LEAD + 32 * i + 32)
                    for j in range(J):
                        last = nc.vector.tensor_scalar(fin[:, u, 0, j], fin[:, u, 0, j], wts[:, 0, ds(n * 4 + j, 1)], None,
                                                       ALU.mult)
                    ch.mark(last)
                    ch.wait()
                    for j in range(J):
                        last = nc.vector.scalar_tensor_tensor(fin[:, u, 0, j], fin[:, u, 1, j], wts[:, 1, ds(n * 4 + j, 1)],
                                                              fin[:, u, 0, j], ALU.mult, ALU.add)
                    ch.mark(last)
                    ch.wait()
                    stats1(lambda j: fin[:, u, 0, j], u, g_var)
                    dve.wait_ge(g_rstd, LEAD + n + 1)
                    for j in range(J):
                        last = nc.vector.tensor_scalar(fin[:, u, 0, j], fin[:, u, 0, j], mv[:, u, j, 0:1],
                                                       rstd[:, u, j:j + 1], ALU.subtract, ALU.mult)
                    ch.mark(last)
                    ch.wait()
                    xc = xl[:, ds(n, 1)].rearrange("p o j d -> p (o j) d")
                    nc.vector.tensor_tensor(xc, xc, fin[:, u, 0], ALU.add).then_inc(g_out, 1)
                ch.end(NB * CH // 2)

        @block.tensor
        def _(pe):
            for each in leading:
                pe.sem_inc(each, LEAD)
            pe.wait_ge(s_const, LEAD + NC)
            nc.tensor.matmul(bank[7][:, 0:NS], wxp[:], wdt[:], start=True, stop=True).then_inc(s_wdt, 1)
            pe.wait_ge(s_wa, LEAD + 1)
            with pe.Fori(0, CH) as c:
                for b in range(NB):
                    pe.wait_ge(a_xn, LEAD + c * 2 + b + 1)
                    pe.wait_ge(a_st, LEAD + c * 2)
                    for j in range(J):
                        last = nc.tensor.transpose(bank[b][:, j * P:(j + 1) * P], xn[:, b, j], ident[:])
                    last.then_inc(a_xt_ps, 1)
                for b in range(NB):
                    pe.wait_ge(a_xt, LEAD + c * 2 + b + 1)
                    pe.wait_ge(a_hc, LEAD + c)
                    last = nc.tensor.matmul(bank[2][:], wa[:, b], xnT[:, b], start=(b == 0), stop=(b == NB - 1))
                last.then_inc(a_proj, 1)
                pe.wait_ge(a_hc, LEAD + c + 1)
                pe.wait_ge(a_yn, LEAD + c * 2)
                for b in range(NB):
                    for j in range(J):
                        y = bank[3 + b][:, j * P:(j + 1) * P]
                        nc.tensor.matmul(y, xnT[:, b, j * P:(j + 1) * P], diagD[:], start=True, stop=False)
                        last = nc.tensor.matmul(y, hc[:, j * P:(j + 1) * P], wout[:, b], start=False, stop=True)
                    last.then_inc(a_y, 1)
                for b in range(NB):
                    pe.wait_ge(a_x1n, LEAD + c * 2 + b + 1)
                    pe.wait_ge(a_x1t, LEAD + c * 2)
                    for j in range(J):
                        last = nc.tensor.transpose(bank[5 + b][:, j * P:(j + 1) * P], row[:, b, j, 0:D], ident[:])
                    last.then_inc(a_x1t_ps, 1)
                for b in range(NB):
                    pe.wait_ge(a_x1t, LEAD + c * 2 + b + 1)
                    for j in range(J):
                        last = nc.tensor.matmul(bank[7][:, 64 * b + j * E0:64 * b + (j + 1) * E0],
                                                x1T[:, b, j * P:(j + 1) * P], wg0[:], start=True, stop=True)
                    last.then_inc(a_sc, 1)
                for b in range(NB):
                    pe.wait_ge(a_row, LEAD + c * 2 + b + 1)
                    for j in range(J):
                        last = nc.tensor.transpose(bank[b][0:E0, j * P:(j + 1) * P], row[:, b, j, D:ROWS], ident[:])
                    last.then_inc(a_st_ps, 1)
            nc_tot = bank[7][:, 0:1]
            pe.wait_ge(c_cnt, LEAD + 1)
            nc.tensor.matmul(nc_tot, blk[:], cntb[:], start=True, stop=True).then_inc(c_tot, 1)
            with pe.Fori(0, 31) as i:
                pe.wait_ge(c_cnt, LEAD + i + 2)
                nc.tensor.matmul(nc_tot, blk[:], cntb[:], start=True, stop=True).then_inc(c_tot, 1)
            pe.wait_ge(c_post, LEAD + 1)
            nc.tensor.matmul(bank[6][:, 0:1], blk[:], cg[:, 0:1], start=True, stop=True)
            nc.tensor.transpose(bank[3][0:1, 0:P], cg[:, 3:4], ident[:]).then_inc(c_mxps, 1)
            nc.tensor.matmul(bank[6][:, 1:2], tri[:], cg[:, 1:2], start=True, stop=True).then_inc(c_postps, 1)
            pe.wait_ge(c_post, LEAD + 2)
            nc.tensor.matmul(bank[6][:, 2:3], tri[:], cg[:, 2:3], start=True, stop=True).then_inc(c_postps, 1)
            pe.wait_ge(c_q, LEAD + 1)
            for w in range(2):
                for h in range(2):
                    last = nc.tensor.transpose(bank[2][:, (2 * w + h) * P:(2 * w + h + 1) * P], qf[:, w, h * P:(h + 1) * P],
                                               ident[:])
            last.then_inc(c_abps, 1)
            pe.wait_ge(c_mx, LEAD + 1)
            nc.tensor.matmul(bank[4][:, 0:1], mrow[:, 1], ones[0:1, 0:1], start=True, stop=True)
            nc.tensor.matmul(bank[5][:, 0:E0], ones[0:1, :], mrow[:, 0, 0:E0], start=True, stop=True).then_inc(c_mxps, 1)
            pe.wait_ge(c_mx, LEAD + 2)
            nc.tensor.matmul(bank[6][:, 8:16], ones[:], wst[:, 1], start=True, stop=True).then_inc(c_mxps, 1)
            pe.wait_ge(c_one, LEAD + 1)
            for t in range(T):
                for n, v in enumerate((valP, valT)):
                    last = nc.tensor.matmul(bank[1][:, 0:256], oneA[:, t].rearrange("p e n -> p (e n)"),
                                            v[:, t].rearrange("p e n -> p (e n)"), start=(t == 0 and n == 0),
                                            stop=(t == T - 1 and n == 1))
            last.then_inc(c_lps, 1)
            pe.wait_ge(s_w0, LEAD + 32)
            pe.wait_ge(c_lst, LEAD + 1)
            with pe.Fori(0, E0) as e:
                def up(k):
                    pe.wait_ge(c_xg[k], e * 16 + 16)
                    pe.wait_ge(c_xt, LEAD + e * 4 + k)
                    nc.tensor.transpose(bank[k % 2][:, 0:P], xg[:, k, 0:D], ident[:]).then_inc(c_xtps, 1)
                    pe.wait_ge(c_xt, LEAD + e * 4 + k + 1)
                    pe.wait_ge(c_gg, LEAD + e * 4 + k)
                    nc.tensor.matmul(bank[2 + k % 2][:], xgT[:, k % 2], w13[:, ds(e, 1)].rearrange("p o n -> p (o n)"),
                                     start=True, stop=True).then_inc(c_h, 1)

                def down(k):
                    pe.wait_ge(c_gg, LEAD + e * 4 + k + 1)
                    for h in range(2):
                        last = nc.tensor.transpose(bank[4 + k % 2][:, h * P:(h + 1) * P], gg[:, k % 2, h * P:(h + 1) * P],
                                                   ident[:])
                    last.then_inc(c_gtps, 1)
                    pe.wait_ge(c_gt, LEAD + e * 4 + k + 1)
                    pe.wait_ge(c_yw, LEAD + e * 4 + k)
                    for h in range(2):
                        last = nc.tensor.matmul(bank[6 + k % 2][:, 0:D], gT[:, k % 2, h * P:(h + 1) * P],
                                                w2[:, ds(e, 1), h].rearrange("p o n -> p (o n)"), start=(h == 0),
                                                stop=(h == 1))
                    last.then_inc(c_y, 1)
                for k in range(4):
                    up(k)
                    down(k)

            pe.wait_ge(d_z, LEAD + 1)
            for b in range(NB):
                if b:
                    pe.wait_ge(d_state, LEAD + b)
                for k in range(3):
                    nc.tensor.matmul(bank[3 + k][:], zerob[:, 0:P], zerob[:], start=True, stop=False, skip_group_check=True)
                with pe.Fori(0, CH // 2) as i:
                    for u in range(2):
                        n = 2 * i + (4 * b + u)
                        pe.wait_ge(d_xh, LEAD + n + 1)
                        pe.wait_ge(d_xt, LEAD + n)
                        for j in range(J):
                            last = nc.tensor.transpose(bank[0][:, j * P:(j + 1) * P], xn[:, u, j], ident[:])
                        last.then_inc(d_xtps, 1)
                        pe.wait_ge(d_xt, LEAD + n + 1)

                        def qkv(j):
                            pe.wait_ge(d_kvb, LEAD + n * 4 + max(j - 1, 0))
                            nc.tensor.matmul(bank[1 + j % 2][:], xnT[:, u, j * P:(j + 1) * P], wqkv[:], start=True,
                                             stop=True).then_inc(d_qkv, 1)

                        def accumulate(j):
                            pe.wait_ge(d_prod, LEAD + n * 4 + (j + 1))
                            kv = kvb[:, j % 2]
                            keys = kc[:, j % 2]

                            def add(o, l, r):
                                return nc.tensor.matmul(o, l, r, start=False, stop=False, skip_group_check=True)
                            for d in range(ND):
                                add(bank[3 + d // 4][:, (d % 4) * P:(d % 4 + 1) * P], prod[:, j % 2, d * P:(d + 1) * P],
                                    kv[:, 1:1 + D])
                            add(bank[5][:, P:2 * P + 1], keys, kv[:, 0:1 + D])
                            add(bank[5][:, 2 * P + 1:3 * P + 1], keys, keys)
                            add(bank[5][:, 3 * P + 1:3 * P + 2], kv[:, 1:1 + D], kv[:, 0:1]).then_inc(d_accum, 1)
                        qkv(0)
                        for j in range(J):
                            if j < J - 1:
                                qkv(j + 1)
                            accumulate(j)
                pe.wait_ge(d_state, LEAD + b + 1)
                with pe.Fori(0, CH) as i:
                    n = i + 4 * b

                    def turn(j):
                        pe.wait_ge(q_prod, LEAD + n * 4 + (j + 1))
                        pe.wait_ge(q_tr, LEAD + (n * 4 + j) * 4)
                        for h in range(3):
                            for k in range((4, 4, 1)[h]):
                                last = nc.tensor.transpose(bank[h][:, k * P:(k + 1) * P],
                                                           prod[:, j % 2, (4 * h + k) * P:(4 * h + k + 1) * P], ident[:])
                            if h == 2:
                                last = nc.tensor.transpose(bank[h][:, P:2 * P], qst[:, j % 2], ident[:])
                            last.then_inc(q_trps, 1)

                    def numerator(j):
                        pe.wait_ge(q_tr, LEAD + (n * 4 + j) * 4 + 4)
                        if j == 0:
                            pe.wait_ge(q_o, LEAD + n)
                        for d in range(ND + 1):
                            last = nc.tensor.matmul(bank[3][:, j * P:(j + 1) * P], smat[:, d],
                                                    prodT[:, j % 2, d * P:(d + 1) * P], start=(d == 0), stop=(d == ND))
                        last.then_inc(q_num, 1)
                    turn(0)
                    for j in range(J):
                        if j < J - 1:
                            turn(j + 1)
                        numerator(j)
                    nc.tensor.matmul(bank[5][:], kk[:], qTg[:], start=True, stop=True).then_inc(q_r, 1)
                    pe.wait_ge(q_t, LEAD + n + 1)
                    nc.tensor.matmul(bank[5][:], halfblk[:], dt_[:], start=True, stop=True).then_inc(q_den, 1)
                    pe.wait_ge(q_o, LEAD + n + 1)
                    pe.wait_ge(q_yn, LEAD + n)
                    for j in range(J):
                        last = nc.tensor.matmul(bank[6][:, j * P:(j + 1) * P], oT[:, j * P:(j + 1) * P], wo[:], start=True,
                                                stop=True)
                    last.then_inc(q_y, 1)
                    pe.wait_ge(q_row, LEAD + n + 1)
                    pe.wait_ge(q_lgc, LEAD + n)
                    for j in range(J):
                        last = nc.tensor.transpose(bank[7][:, j * P:(j + 1) * P], row[:, 0, j, 0:D], ident[:])
                    last.then_inc(q_rtps, 1)
                    pe.wait_ge(q_rt, LEAD + n + 1)
                    for j in range(J):
                        last = nc.tensor.matmul(bank[7][:, j * E1:(j + 1) * E1], x1T[:, 0, j * P:(j + 1) * P], wr[:], start=True,
                                                stop=True)
                    last.then_inc(q_lg, 1)
            pe.wait_ge(r_both, LEAD + 1)
            rhs = both[:].rearrange("p e t -> p (e t)")
            nc.tensor.matmul(bank[1][:, 0:256], tri128[:], rhs, start=True, stop=True).then_inc(r_ps, 1)
            nc.tensor.matmul(bank[2][:, 0:256], ones[:], rhs, start=True, stop=True).then_inc(r_ps, 1)
            nc.tensor.matmul(bank[3][:], zerob[:, 0:P], zerob[:], start=True, stop=False, skip_group_check=True)
            with pe.Fori(0, T) as t:
                for c in range(2):
                    pe.wait_ge(r_one, LEAD + t * 2 + (c + 1))
                    nc.tensor.matmul(bank[3][:, 0:2 * NT], oneLo2[:, c], oneV.rearrange("p (c n) -> p c n", c=2)[:, c],
                                     start=False, stop=False, skip_group_check=True).then_inc(r_slot, 1)
            pe.wait_ge(r_fti, LEAD + 1)
            pe.wait_ge(s_w1, LEAD + 32)
            pe.wait_ge(r_idx, LEAD + 1)
            def experts(at):
                n, m, o, l = at(1), at(0), at(-1), at(-2)
                if n:
                    pe.wait_ge(f_x[n.ring], 16 * n.lap + 16)
                    if not (isinstance(n.t, int) and n.t < 2):
                        pe.wait_ge(f_xt, LEAD + n.t - 1)
                    nc.tensor.transpose(bank[(0, 7)[n.pair]][:, 0:D], xr[:, n.ring], ident[:]).then_inc(f_xtps, 1)
                if m:
                    e = pe.value_load(fti[0:1, ds(m.t, 1)], min_val=0, max_val=E1 - 1)
                    pe.wait_ge(f_xt, LEAD + m.t + 1)
                    if not (isinstance(m.t, int) and m.t < 2):
                        pe.wait_ge(f_g, LEAD + m.t - 1)
                    nc.tensor.matmul(bank[1 + m.pair][:], xrT[:, m.pair], wgu[:, ds(e, 1), 0:H1].rearrange("p o n -> p (o n)"),
                                     start=True, stop=True).then_inc(f_gu, 1)
                    nc.tensor.matmul(bank[3 + m.pair][:], xrT[:, m.pair], wgu[:, ds(e, 1), H1:].rearrange("p o n -> p (o n)"),
                                     start=True, stop=True).then_inc(f_up, 1)
                if o:
                    pe.wait_ge(f_g, LEAD + o.t + 1)
                    if not (isinstance(o.t, int) and o.t < 1):
                        pe.wait_ge(f_gt, LEAD + o.t)
                    for h in range(4):
                        last = nc.tensor.transpose(bank[5][:, h * P:(h + 1) * P], gl[:, o.pair, h * P:(h + 1) * P], ident[:])
                    last.then_inc(f_gtps, 1)
                if l:
                    e = pe.value_load(fti[0:1, ds(l.t, 1)], min_val=0, max_val=E1 - 1)
                    pe.wait_ge(f_gt, LEAD + l.t + 1)
                    if not (isinstance(l.t, int) and l.t < 1):
                        pe.wait_ge(f_yr, LEAD + l.t)
                    for h in range(4):
                        last = nc.tensor.matmul(bank[6][:, 0:D], glT[:, l.pair, h * P:(h + 1) * P],
                                                wd[:, ds(e, 1), h].rearrange("p o n -> p (o n)"), start=(h == 0), stop=(h == 3))
                    last.then_inc(f_y, 1)
            pipeline(pe, experts, 1, 2)


def kernel(**inputs):
    import concourse.bacc as _bacc
    from concourse.bass_utils import run_bass_kernel_spmd as _run

    g = {k: np.asarray(v) for k, v in inputs.items()}
    wxp = g["L0_attn_Wxproj"]
    wa = np.zeros((D, NB, P), np.float32)
    for b in range(NB):
        for q, w in ((1, wxp[64:64 + NS]), (2, wxp[64 + NS:]), (3, g["L0_attn_Wxs"])):
            wa[:, b, 32 * q + NS * b:32 * q + NS * (b + 1)] = w.T
    wout = np.zeros((32, NB, D), np.float32)
    for b in range(NB):
        wout[NS * b:NS * (b + 1), b] = g["L0_attn_Wout"].T
    wrap = np.concatenate([np.arange(DH), np.arange(KW - DH)])
    heads = lambda w: w.reshape(D, HD, DH)[:, :, wrap].reshape(D, HD * KW)
    wkv = g["L1_attn_w_kv"]
    wqkv = np.concatenate([wkv[:, D:], heads(wkv[:, :D]), heads(g["L1_attn_w_q"])], axis=1)
    arrays = {
        "x": g["L0_attn_x"].reshape(T * P, D),
        "wa": wa,
        "wxp": wxp[:64],
        "wdt": np.repeat(g["L0_attn_Wdt"].T, NS, axis=1),
        "bdt": np.repeat(g["L0_attn_bdt"][None], 32, axis=0),
        "alog": np.concatenate([g["L0_attn_A_log"].T] * NB, axis=0),
        "wout": wout,
        "dp": g["L0_attn_Dp"][:, None],
        "ident": np.eye(P, dtype=np.float32),
        "wg0": g["L0_ffn_Wg"].T,
        "blk": np.kron(np.eye(E0), np.ones((16, 16))).astype(np.float32),
        "tri": np.kron(np.eye(E0), np.triu(np.ones((16, 16)), 1)).astype(np.float32),
        "bits": np.repeat(np.array([[1 << (30 - i) for i in range(31)] + [0]], np.uint32), P, axis=0),
        "iota": np.repeat(np.arange(32, dtype=np.float32)[None], P, axis=0),
        "pcol": np.arange(P, dtype=np.float32)[:, None],
        "tile128": np.repeat(P * np.arange(T, dtype=np.float32)[None], P, axis=0),
        "emask": np.repeat(np.eye(E0, dtype=np.float32), 16, axis=0),
        "w13": np.concatenate([g["L0_ffn_W1"], g["L0_ffn_W3"]], axis=1).transpose(2, 0, 1),
        "wqkv": wqkv,
        "gamma": g["L1_attn_gamma"][:, None],
        "wo": g["L1_attn_w_out"],
        "wr": g["L1_ffn_Wr"],
        "wgu": np.concatenate([g["L1_ffn_Wg"], g["L1_ffn_Wu"]], axis=2).transpose(1, 0, 2),
        "wd": g["L1_ffn_Wd"].reshape(E1, 4, P, D).transpose(2, 0, 1, 3),
        "tri128": np.triu(np.ones((P, P)), 1).astype(np.float32),
        "iota_t": np.repeat(np.arange(P, dtype=np.float32)[None], P, axis=0),
        "slot_pad": (2 * T * P + np.arange(NT)[None] * P + np.arange(P)[:, None]).astype(np.float32),
        "choice128": np.repeat((np.arange(T)[None] + T * np.arange(2)[:, None] - 2 * T).astype(np.float32)[None] * P, P, axis=0),
        "rev8": np.repeat(np.arange(E1, 0, -1, dtype=np.float32)[None], P, axis=0),
        "w2": g["L0_ffn_W2"].reshape(E0, D, 2, P).transpose(3, 0, 2, 1),
    }
    nc = _bacc.Bacc("TRN2", target_bir_lowering=False, num_devices=1)
    feed, inp = {}, {}
    for name, a in arrays.items():
        a = np.ascontiguousarray(a)
        feed[f"in_{name}"] = a
        inp[name] = nc.dram_tensor(f"in_{name}", a.shape, mybir.dt.from_np(a.dtype), kind="ExternalInput").ap()
    out = nc.dram_tensor("out_0", (T * P, D), F32, kind="ExternalOutput").ap()
    program(nc, inp, [out])
    r = _run(nc, [feed], core_ids=[0])
    return r.results[0]["out_0"].reshape(NB, L, D)
```
